# Optimizing a Trainium2 kernel written in Bass

```python
import numpy as np
import jax
import jax.numpy as jnp

def _softmax(x, axis=-1):
    return jax.nn.softmax(x, axis=axis)

def _gelu(x):
    return jax.nn.gelu(x, approximate=True)

def _silu(x):
    return jax.nn.silu(x)

def _sigmoid(x):
    return jax.nn.sigmoid(x)

def _layernorm(x, axis=-1, eps=1e-05):
    m = jnp.mean(x, axis=axis, keepdims=True)
    v = jnp.var(x, axis=axis, keepdims=True)
    return (x - m) / jnp.sqrt(v + eps)

def _scatter_add(tgt, idx, src, axis=0):
    return tgt.at[idx].add(src)

def _segment_sum(src, seg, n):
    return jax.ops.segment_sum(src, seg, n)
kernel_name = 'mk_dlrm_tower_d1_rec_r8_282c28'

def setup_inputs(seed: int=0):
    np.random.seed(seed)
    _w = jnp.asarray

    def _rec_inputs():
        import jax
        import jax.numpy as jnp
        _tk = jax.random.key(seed)
        ids = jnp.stack([jax.random.randint(jax.random.fold_in(_tk, 200 + f), (2048,), 0, v, jnp.int32) for f, v in enumerate([1250, 1250, 125000, 1000, 1000, 1000, 12500, 1250, 1000, 1250, 1000, 1000, 1250, 12500, 1250, 12500, 1000, 1250, 1000, 1250, 12500, 1000, 1000, 12500, 1250, 12500])], axis=1)
        tbl_0 = 0.05 * jax.random.normal(jax.random.fold_in(_tk, 500 + 0), (1250, 128), jnp.float32)
        tbl_1 = 0.05 * jax.random.normal(jax.random.fold_in(_tk, 500 + 1), (1250, 128), jnp.float32)
        tbl_2 = 0.05 * jax.random.normal(jax.random.fold_in(_tk, 500 + 2), (125000, 128), jnp.float32)
        tbl_3 = 0.05 * jax.random.normal(jax.random.fold_in(_tk, 500 + 3), (1000, 128), jnp.float32)
        tbl_4 = 0.05 * jax.random.normal(jax.random.fold_in(_tk, 500 + 4), (1000, 128), jnp.float32)
        tbl_5 = 0.05 * jax.random.normal(jax.random.fold_in(_tk, 500 + 5), (1000, 128), jnp.float32)
        tbl_6 = 0.05 * jax.random.normal(jax.random.fold_in(_tk, 500 + 6), (12500, 128), jnp.float32)
        tbl_7 = 0.05 * jax.random.normal(jax.random.fold_in(_tk, 500 + 7), (1250, 128), jnp.float32)
        tbl_8 = 0.05 * jax.random.normal(jax.random.fold_in(_tk, 500 + 8), (1000, 128), jnp.float32)
        tbl_9 = 0.05 * jax.random.normal(jax.random.fold_in(_tk, 500 + 9), (1250, 128), jnp.float32)
        tbl_10 = 0.05 * jax.random.normal(jax.random.fold_in(_tk, 500 + 10), (1000, 128), jnp.float32)
        tbl_11 = 0.05 * jax.random.normal(jax.random.fold_in(_tk, 500 + 11), (1000, 128), jnp.float32)
        tbl_12 = 0.05 * jax.random.normal(jax.random.fold_in(_tk, 500 + 12), (1250, 128), jnp.float32)
        tbl_13 = 0.05 * jax.random.normal(jax.random.fold_in(_tk, 500 + 13), (12500, 128), jnp.float32)
        tbl_14 = 0.05 * jax.random.normal(jax.random.fold_in(_tk, 500 + 14), (1250, 128), jnp.float32)
        tbl_15 = 0.05 * jax.random.normal(jax.random.fold_in(_tk, 500 + 15), (12500, 128), jnp.float32)
        tbl_16 = 0.05 * jax.random.normal(jax.random.fold_in(_tk, 500 + 16), (1000, 128), jnp.float32)
        tbl_17 = 0.05 * jax.random.normal(jax.random.fold_in(_tk, 500 + 17), (1250, 128), jnp.float32)
        tbl_18 = 0.05 * jax.random.normal(jax.random.fold_in(_tk, 500 + 18), (1000, 128), jnp.float32)
        tbl_19 = 0.05 * jax.random.normal(jax.random.fold_in(_tk, 500 + 19), (1250, 128), jnp.float32)
        tbl_20 = 0.05 * jax.random.normal(jax.random.fold_in(_tk, 500 + 20), (12500, 128), jnp.float32)
        tbl_21 = 0.05 * jax.random.normal(jax.random.fold_in(_tk, 500 + 21), (1000, 128), jnp.float32)
        tbl_22 = 0.05 * jax.random.normal(jax.random.fold_in(_tk, 500 + 22), (1000, 128), jnp.float32)
        tbl_23 = 0.05 * jax.random.normal(jax.random.fold_in(_tk, 500 + 23), (12500, 128), jnp.float32)
        tbl_24 = 0.05 * jax.random.normal(jax.random.fold_in(_tk, 500 + 24), (1250, 128), jnp.float32)
        tbl_25 = 0.05 * jax.random.normal(jax.random.fold_in(_tk, 500 + 25), (12500, 128), jnp.float32)
        _rk = jax.random.fold_in(_tk, 7)
        r_dense_features = -0.000292821 + 1.00034 * jax.random.normal(jax.random.fold_in(_rk, 101), (2048, 128), jnp.float32)
        W_top1 = 0.0405887 * jax.random.normal(jax.random.fold_in(_tk, 801), (607, 512), jnp.float32)
        W_top2 = 0.0441942 * jax.random.normal(jax.random.fold_in(_tk, 802), (512, 256), jnp.float32)
        W_top3 = 0.0625 * jax.random.normal(jax.random.fold_in(_tk, 803), (256, 1), jnp.float32)
        b_top1 = jnp.zeros((512,), jnp.float32)
        b_top2 = jnp.zeros((256,), jnp.float32)
        return (r_dense_features, ids, tbl_0, tbl_1, tbl_2, tbl_3, tbl_4, tbl_5, tbl_6, tbl_7, tbl_8, tbl_9, tbl_10, tbl_11, tbl_12, tbl_13, tbl_14, tbl_15, tbl_16, tbl_17, tbl_18, tbl_19, tbl_20, tbl_21, tbl_22, tbl_23, tbl_24, tbl_25, W_top1, b_top1, W_top2, b_top2, W_top3)
    r_dense_features, ids, tbl_0, tbl_1, tbl_2, tbl_3, tbl_4, tbl_5, tbl_6, tbl_7, tbl_8, tbl_9, tbl_10, tbl_11, tbl_12, tbl_13, tbl_14, tbl_15, tbl_16, tbl_17, tbl_18, tbl_19, tbl_20, tbl_21, tbl_22, tbl_23, tbl_24, tbl_25, W_top1, b_top1, W_top2, b_top2, W_top3 = _rec_inputs()

    def _L0_rec_setup():
        import jax, jax.numpy as jnp
        import numpy as np
        F = 26
        _TRIU_I, _TRIU_J = np.triu_indices(F + 1, k=1)
        key = jax.random.key(seed)
        k1, k2 = jax.random.split(key)
        B, D = (4096, 128)
        dense_features = jax.random.normal(k1, (B, D), dtype=jnp.float32)
        sparse_features = jax.random.normal(k2, (B, F, D), dtype=jnp.float32)
        return {'dense_features': dense_features, 'sparse_features': sparse_features}
    _L0_rec_all = _L0_rec_setup()
    _L0_rec_in = {k: v for k, v in _L0_rec_all.items() if k in ()}
    del _L0_rec_all
    return {'r_dense_features': r_dense_features, 'ids': ids, 'tbl_0': tbl_0, 'tbl_1': tbl_1, 'tbl_2': tbl_2, 'tbl_3': tbl_3, 'tbl_4': tbl_4, 'tbl_5': tbl_5, 'tbl_6': tbl_6, 'tbl_7': tbl_7, 'tbl_8': tbl_8, 'tbl_9': tbl_9, 'tbl_10': tbl_10, 'tbl_11': tbl_11, 'tbl_12': tbl_12, 'tbl_13': tbl_13, 'tbl_14': tbl_14, 'tbl_15': tbl_15, 'tbl_16': tbl_16, 'tbl_17': tbl_17, 'tbl_18': tbl_18, 'tbl_19': tbl_19, 'tbl_20': tbl_20, 'tbl_21': tbl_21, 'tbl_22': tbl_22, 'tbl_23': tbl_23, 'tbl_24': tbl_24, 'tbl_25': tbl_25, 'W_top1': W_top1, 'b_top1': b_top1, 'W_top2': W_top2, 'b_top2': b_top2, 'W_top3': W_top3}

def reference(r_dense_features, ids, tbl_0, tbl_1, tbl_2, tbl_3, tbl_4, tbl_5, tbl_6, tbl_7, tbl_8, tbl_9, tbl_10, tbl_11, tbl_12, tbl_13, tbl_14, tbl_15, tbl_16, tbl_17, tbl_18, tbl_19, tbl_20, tbl_21, tbl_22, tbl_23, tbl_24, tbl_25, W_top1, b_top1, W_top2, b_top2, W_top3):
    import jax
    import jax.numpy as jnp

    def _L0_rec_ref(dense_features, sparse_features):
        import jax, jax.numpy as jnp
        import numpy as np
        F = 26
        _TRIU_I, _TRIU_J = np.triu_indices(F + 1, k=1)
        combined = jnp.concatenate([dense_features[:, None, :], sparse_features], axis=1)
        interactions = jnp.einsum('bfd,bgd->bfg', combined, combined)
        interactions_flat = interactions[:, _TRIU_I, _TRIU_J]
        return jnp.concatenate([dense_features, interactions_flat], axis=1)
    e = jnp.stack([tbl_0[ids[:, 0]], tbl_1[ids[:, 1]], tbl_2[ids[:, 2]], tbl_3[ids[:, 3]], tbl_4[ids[:, 4]], tbl_5[ids[:, 5]], tbl_6[ids[:, 6]], tbl_7[ids[:, 7]], tbl_8[ids[:, 8]], tbl_9[ids[:, 9]], tbl_10[ids[:, 10]], tbl_11[ids[:, 11]], tbl_12[ids[:, 12]], tbl_13[ids[:, 13]], tbl_14[ids[:, 14]], tbl_15[ids[:, 15]], tbl_16[ids[:, 16]], tbl_17[ids[:, 17]], tbl_18[ids[:, 18]], tbl_19[ids[:, 19]], tbl_20[ids[:, 20]], tbl_21[ids[:, 21]], tbl_22[ids[:, 22]], tbl_23[ids[:, 23]], tbl_24[ids[:, 24]], tbl_25[ids[:, 25]]], axis=1)
    z = _L0_rec_ref(r_dense_features, e)
    z = z.reshape(z.shape[0], -1)
    h = jnp.concatenate([z, r_dense_features], axis=1)
    h = jnp.maximum(h @ W_top1 + b_top1, 0.0)
    h = jnp.maximum(h @ W_top2 + b_top2, 0.0)
    y = h @ W_top3
    return y

_drawn_inputs = setup_inputs


def setup_inputs(seed=0):
    import zlib

    import numpy as np

    out = dict(_drawn_inputs(seed))
    spreads = {'b_top1': (0.0, 0.1), 'b_top2': (0.0, 0.1)}
    factors = {}
    for name, (base, spread) in spreads.items():
        noise = np.random.default_rng([zlib.crc32(name.encode()), seed]).standard_normal(out[name].shape)
        drawn = base * np.exp(spread * noise) if base else spread * noise
        out[name] = jnp.asarray(drawn.astype(out[name].dtype))
    for name, factor in factors.items():
        out[name] = (out[name] * factor).astype(out[name].dtype)
    return out
```

```python
from contextlib import ExitStack

import numpy as np
import concourse.bass as bass
from concourse import mybir

F32 = mybir.dt.float32
I32 = mybir.dt.int32
ALU = mybir.AluOpType
ACT = mybir.ActivationFunctionType

B, D, NF = 2048, 128, 27
NE = NF - 1
P = 128
TILES = B // P
SLOTS = 32
NJ = NF - 1
Q, G = 4, P // 4
N1, N2 = 512, 256
PER_GROUP = 4
GROUPS = [range(a, min(a + PER_GROUP, NF)) for a in range(0, NF, PER_GROUP)]
NG = len(GROUPS)
UNITS = 4
UG = G // UNITS
BG = UG // 2
RECTS = []
_at = 0
for _s in range(0, NJ, 3):
    _c = min(3, NJ - _s)
    RECTS.append((_s, _c, min(_s + 3, NJ), _at))
    _at += _c * RECTS[-1][2]
PAIRS = _at
KP = -(-PAIRS // P)
K1, K2 = KP + 1, N1 // P
M1, M2 = N1 // P, N2 // P
LOADS = 7


def pair_rows():
    rows = np.full(KP * P, -1, np.int64)
    for s, c, r, off in RECTS:
        for a in range(c):
            for i in range(r):
                j = s + a + 1
                if i < j:
                    rows[off + a * r + i] = D + i * NF - i * (i + 1) // 2 + j - i - 1
    return rows


def build(nc, dense, ids, tables, w1p, w1a, w1b, b1, w2, b2, w3, out):
    with ExitStack() as ctx:
        def sb(name, shape, dt=F32):
            return ctx.enter_context(nc.sbuf_tensor(name, shape, dt))

        def sem(name):
            return ctx.enter_context(nc.semaphore(name))

        ident = sb("ident", [P, P])
        ids_sb = sb("ids_sb", [P, 2, NE], I32)
        emb = sb("emb", [P, 2, NF, D])
        xt = sb("xt", [P, 2, G, Q, SLOTS])
        dense_t = sb("dense_t", [P, 2, P])
        blocks = sb("blocks", [P, 2, G, NJ])
        turned = sb("turned", [P, NJ, SLOTS])
        pairs = sb("pairs", [P, 2, KP * P])
        pairs_t = sb("pairs_t", [P, KP, P])
        h1 = sb("h1", [P, M1, P])
        h2 = sb("h2", [P, M2, P])
        y_sb = sb("y_sb", [1, 2, P])
        w1_sb = sb("w1_sb", [P, K1, N1])
        w1b_sb = sb("w1b_sb", [P, N1])
        w2_sb = sb("w2_sb", [P, K2, N2])
        w3_sb = sb("w3_sb", [P, M2])
        b1_sb = sb("b1_sb", [P, M1])
        b2_sb = sb("b2_sb", [P, M2])

        pt = [ctx.enter_context(nc.psum_tensor(f"pt{k}", [P, PER_GROUP, P], F32)) for k in range(2)]
        pgram = ctx.enter_context(nc.psum_tensor("pgram", [P, 4, 512], F32))
        pmix = ctx.enter_context(nc.psum_tensor("pmix", [P, 512], F32))
        ph1 = ctx.enter_context(nc.psum_tensor("ph1", [P, M1, P], F32))
        ppairs = pmix[:, 0:KP * P].rearrange("p (k s) -> p k s", k=KP)
        ph2 = pmix[:, 0:N2].rearrange("p (m s) -> p m s", m=M2)
        py = pmix[0:1, KP * P:KP * P + P]

        s_zero = sem("s_zero")
        s_ident = sem("s_ident")
        s_weights = sem("s_weights")
        s_pads = sem("s_pads")
        s_w1 = sem("s_w1")
        s_ids = [sem(f"s_ids{k}") for k in range(2)]
        s_dense = [sem(f"s_dense{k}") for k in range(2)]
        s_rows = [[sem(f"s_rows{k}_{g}") for g in range(NG)] for k in range(2)]
        s_go = sem("s_go")
        s_turned = sem("s_turned")
        s_xt = [sem("s_xt_dve"), sem("s_xt_act")]
        s_dt = sem("s_dt")
        s_gram = sem("s_gram")
        s_blk = [sem("s_blk_dve"), sem("s_blk_act")]
        s_flip = sem("s_flip")
        s_pick = [sem("s_pick_dve"), sem("s_pick_act")]
        s_pp = sem("s_pp")
        s_pe = sem("s_pe")
        s_l1 = sem("s_l1")
        s_r1 = sem("s_r1")
        s_l2 = sem("s_l2")
        s_r2 = sem("s_r2")
        s_l3 = sem("s_l3")
        s_y = sem("s_y")
        s_out = [sem("s_out0"), sem("s_out1")]

        block = ctx.enter_context(nc.Block())

        def steps(eng, step):
            step(0, 0, True, False, False)
            step(0, 1, True, True, False)
            step(1, 0, True, True, True)
            step(1, 1, True, True, True)
            with eng.Fori(2, TILES // 2) as i:
                step(i, 0, True, True, True)
                step(i, 1, True, True, True)
            step(TILES // 2, 0, False, True, True)
            step(TILES // 2, 1, False, False, True)

        def back(i, k, n):
            return i + (k - n) // 2, (k - n) % 2

        def wait(eng, s, value):
            if not isinstance(value, int) or value > 0:
                eng.wait_ge(s, value)

        def copied(i, k, g, parity):
            return NG * i + (NG * k + g - parity) // 2 + 1

        @block.sync
        def _(sp):
            def load(i, k):
                if not isinstance(i, int) or i > 0:
                    sp.wait_ge(s_turned, NG * (2 * i + k - 1))
                sp.dma_start(ids_sb[:, k, :], ids[bass.ts(2 * i + k, P), :]).then_inc(s_ids[k], 16)
                sp.dma_start(emb[:, k, 0, :], dense[bass.ts(2 * i + k, P), :]).then_inc(s_dense[k], 16)

            def store(i, k):
                sp.wait_ge(s_y, 2 * i + k + 1)
                sp.dma_start(out[bass.ts(2 * i + k, P), :].rearrange("s o -> o s"),
                             y_sb[:, k, :]).then_inc(s_out[k], 16)

            load(0, 0)
            load(0, 1)
            load(1, 0)
            load(1, 1)
            store(0, 0)
            with sp.Fori(2, TILES // 2) as i:
                load(i, 0)
                store(i - 2, 1)
                load(i, 1)
                store(i - 1, 0)
            store(TILES // 2 - 2, 1)
            store(TILES // 2 - 1, 0)
            store(TILES // 2 - 1, 1)
            for s in s_out:
                sp.wait_ge(s, 16 * (TILES // 2))

        @block.gpsimd
        def _(pool):
            pool.memset(ident[:], 0.0).then_inc(s_zero, 1)
            pool.wait_ge(s_zero, 1)
            pool.affine_select(out=ident[:], in_=ident[:], compare_op=ALU.not_equal, fill=1.0, base=0,
                               pattern=[[-1, P]], channel_multiplier=1).then_inc(s_ident, 1)

            def gather(i, k):
                pool.wait_ge(s_ids[k], 16 * (i + 1))
                pool.sem_inc(s_go, 1)
                for g, group in enumerate(GROUPS):
                    if not isinstance(i, int) or i > 0:
                        pool.wait_ge(s_turned, NG * (2 * i + k - 2) + g + 1)
                        pool.sem_inc(s_go, 1)
                    for f in group:
                        if f:
                            pool.indirect_dma_start(
                                out=emb[:, k, f, :], out_offset=None, in_=tables[f - 1],
                                in_offset=bass.IndirectOffsetOnAxis(ap=ids_sb[:, k, f - 1:f], axis=0),
                            ).then_inc(s_rows[k][g], 16)

            gather(0, 0)
            gather(0, 1)
            with pool.Fori(1, TILES // 2) as i:
                gather(i, 0)
                gather(i, 1)

        @block.tensor
        def _(pe):
            def turn(i, k, g):
                n = NG * k + g
                group = GROUPS[g]
                pe.wait_ge(s_rows[k][g], 16 * sum(f > 0 for f in group) * (i + 1))
                if g == 0:
                    pe.wait_ge(s_dense[k], 16 * (i + 1))
                wait(pe, s_xt[n % 2], NG * i + n // 2)
                for c, f in enumerate(group):
                    last = pe.transpose(pt[n % 2][:, c, :], emb[:, k, f, :], ident[:])
                last.then_inc(s_turned, 1)

            def gram(i, k, u):
                if u == 0:
                    pe.wait_ge(s_xt[0], copied(i, k, NG - 1, 0))
                    pe.wait_ge(s_xt[1], copied(i, k, NG - 1, 1))
                for s in s_blk:
                    wait(pe, s, UNITS * (2 * i + k) + u - 1)
                for c in range(UG):
                    bank = 2 * (u % 2) + c // BG
                    at = (c % BG) * Q * NJ
                    four = xt[:, k, u * UG + c, :, :]
                    last = pe.matmul(pgram[:, bank, at:at + Q * NJ], four.rearrange("p q f -> p (q f)"),
                                     four[:, :, 1:NF], start=True, stop=True)
                last.then_inc(s_gram, 1)

            def turn_pairs(i, k):
                for s in s_pick:
                    pe.wait_ge(s, 2 * i + k + 1)
                wait(pe, s_y, 2 * i + k)
                for c in range(KP):
                    last = pe.transpose(ppairs[:, c, :], pairs[:, k, bass.ts(c, P)], ident[:])
                last.then_inc(s_pp, 1)

            def layer1(i, k):
                pe.wait_ge(s_pe, 2 * i + k + 1)
                pe.wait_ge(s_dt, 2 * i + k + 1)
                for m in range(M1):
                    for c in range(K1):
                        rhs = pairs_t[:, c, :] if c < KP else dense_t[:, k, :]
                        last = pe.matmul(ph1[:, m, :], w1_sb[:, c, bass.ts(m, P)], rhs,
                                         start=(c == 0), stop=(c == K1 - 1))
                last.then_inc(s_l1, 1)

            def layer2(i, k):
                pe.wait_ge(s_r1, 2 * i + k + 1)
                for m in range(M2):
                    for c in range(K2):
                        last = pe.matmul(ph2[:, m, :], w2_sb[:, c, bass.ts(m, P)], h1[:, c, :],
                                         start=(c == 0), stop=(c == K2 - 1))
                last.then_inc(s_l2, 1)

            def layer3(i, k):
                pe.wait_ge(s_r2, 2 * i + k + 1)
                for c in range(M2):
                    last = pe.matmul(py, w3_sb[:, c:c + 1], h2[:, c, :], start=(c == 0), stop=(c == M2 - 1))
                last.then_inc(s_l3, 1)

            def step(i, k, tile, gram_, mlp):
                for g in range(NG):
                    if tile:
                        turn(i, k, g)
                    if gram_ and g < UNITS:
                        gram(*back(i, k, 1), g)
                    if mlp and g == 0:
                        turn_pairs(*back(i, k, 2))
                    if mlp and g == 2:
                        layer1(*back(i, k, 2))
                    if mlp and g == 4:
                        layer2(*back(i, k, 2))
                    if mlp and g == 6:
                        layer3(*back(i, k, 2))

            pe.wait_ge(s_ident, 1)
            pe.wait_ge(s_pads, 3)
            pe.wait_ge(s_weights, 16 * LOADS)
            pe.wait_ge(s_w1, 1)
            steps(pe, step)

        def copy_group(eng, copy, i, k, g, parity):
            group = GROUPS[g]
            eng.wait_ge(s_turned, NG * (2 * i + k) + g + 1)
            if g < 2 and (not isinstance(i, int) or i > 0):
                eng.wait_ge(s_gram, UNITS * (2 * i + k - 1))
                eng.wait_ge(s_dt, 2 * i + k - 1)
            copy(xt[:, k, :, :, group[0]:group[-1] + 1].rearrange("p g q f -> p q g f"),
                 pt[parity][:, 0:len(group), :].rearrange("p f (q g) -> p q g f", q=Q)).then_inc(s_xt[parity], 1)

        def copy_blocks(eng, copy, i, k, u, half):
            eng.wait_ge(s_gram, UNITS * (2 * i + k) + u + 1)
            if u == 0:
                wait(eng, s_flip, 2 * i + k - 1)
            for q in (2 * half, 2 * half + 1):
                rows = slice(SLOTS * q, SLOTS * q + SLOTS)
                src = pgram[rows, 2 * (u % 2):2 * (u % 2) + 2, 0:BG * Q * NJ]
                src = src.rearrange("p b (c q j) -> p b c q j", c=BG, q=Q)[:, :, :, q, :]
                dst = blocks[rows, k, u * UG:(u + 1) * UG, :].rearrange("p (b c) j -> p b c j", b=2)
                last = copy(dst, src)
            last.then_inc(s_blk[half], 1)

        def pick(eng, copy, i, k, rects, engine):
            eng.wait_ge(s_flip, 2 * i + k + 1)
            wait(eng, s_pp, 2 * i + k - 1)
            for s, c, r, off in rects:
                last = copy(pairs[:, k, off:off + c * r].rearrange("p (c r) -> p c r", c=c),
                            turned[:, s:s + c, 0:r])
            last.then_inc(s_pick[engine], 1)

        @block.vector
        def _(dve):
            def copy(dst, src):
                return dve.tensor_copy(dst, src)

            def flip(i, k):
                for s in s_blk:
                    dve.wait_ge(s, UNITS * (2 * i + k + 1))
                for s in s_pick:
                    wait(dve, s, 2 * i + k)
                dve.transpose(turned[:], blocks[:, k, :, :].rearrange("p g j -> p j g")).then_inc(s_flip, 1)

            def copy_dense(i, k):
                for s in range(2):
                    dve.wait_ge(s_xt[s], copied(i, k, NG - 1, s))
                wait(dve, s_l1, 2 * i + k - 1)
                copy(dense_t[:, k, :].rearrange("p (q g) -> p q g", q=Q),
                     xt[:, k, :, :, 0].rearrange("p g q -> p q g")).then_inc(s_dt, 1)

            def relu2(i, k):
                dve.wait_ge(s_l2, 2 * i + k + 1)
                wait(dve, s_l3, 2 * i + k)
                for m in range(M2):
                    last = dve.tensor_scalar(h2[:, m, :], ph2[:, m, :], b2_sb[:, m:m + 1], 0.0, ALU.add, ALU.max)
                last.then_inc(s_r2, 1)

            def put_y(i, k):
                dve.wait_ge(s_l3, 2 * i + k + 1)
                wait(dve, s_out[k], 16 * i)
                copy(y_sb[:, k, :], py).then_inc(s_y, 1)

            def step(i, k, tile, gram, mlp):
                for g in range(NG):
                    if tile and (NG * k + g) % 2 == 0:
                        copy_group(dve, copy, i, k, g, 0)
                    if gram and g < UNITS:
                        copy_blocks(dve, copy, *back(i, k, 1), g, 0)
                    if gram and g == 4:
                        flip(*back(i, k, 1))
                    if gram and g == 5:
                        pick(dve, copy, *back(i, k, 1), RECTS[0::2], 0)
                        copy_dense(*back(i, k, 1))
                    if mlp and g == 4:
                        relu2(*back(i, k, 2))
                    if mlp and g == 6:
                        put_y(*back(i, k, 2))

            dve.memset(xt[:, :, :, :, NF:SLOTS].rearrange("p k g q f -> p (k g q) f"), 0.0).then_inc(s_pads, 1)
            for k in range(2):
                dve.memset(pairs[:, k, PAIRS:KP * P], 0.0).then_inc(s_pads, 1)
            dve.wait_ge(s_weights, 16 * LOADS)
            dve.tensor_tensor(w1_sb[:, KP, :], w1_sb[:, KP, :], w1b_sb[:], ALU.add).then_inc(s_w1, 1)
            steps(dve, step)

        @block.scalar
        def _(act):
            def copy(dst, src):
                return act.activation(dst, src, ACT.Copy)

            def copy_pairs(i, k):
                act.wait_ge(s_pp, 2 * i + k + 1)
                wait(act, s_l1, 2 * i + k)
                copy(pairs_t[:], ppairs).then_inc(s_pe, 1)

            def relu1(i, k):
                act.wait_ge(s_l1, 2 * i + k + 1)
                wait(act, s_l2, 2 * i + k)
                for m in range(M1):
                    last = act.activation(h1[:, m, :], ph1[:, m, :], ACT.Relu, bias=b1_sb[:, m:m + 1])
                last.then_inc(s_r1, 1)

            def step(i, k, tile, gram, mlp):
                for g in range(NG):
                    if tile and (NG * k + g) % 2 == 1:
                        copy_group(act, copy, i, k, g, 1)
                    if gram and g < UNITS:
                        copy_blocks(act, copy, *back(i, k, 1), g, 1)
                    if mlp and g == 0:
                        copy_pairs(*back(i, k, 2))
                    if mlp and g == 2:
                        relu1(*back(i, k, 2))
                    if gram and g == 5:
                        pick(act, copy, *back(i, k, 1), RECTS[1::2], 1)

            loads = [(w1_sb[:, 0:KP, :], w1p.rearrange("(c p) n -> p c n", p=P)),
                     (w1_sb[:, KP, :], w1a), (w1b_sb[:], w1b),
                     (w2_sb[:], w2.rearrange("(c p) n -> p c n", p=P)),
                     (w3_sb[:], w3), (b1_sb[:], b1), (b2_sb[:], b2)]
            assert len(loads) == LOADS
            for dst, src in loads:
                act.dma_start(dst, src).then_inc(s_weights, 16)
            act.wait_ge(s_weights, 16 * LOADS)
            steps(act, step)


def kernel(**inputs):
    import concourse.bacc as bacc
    from concourse.bass_utils import run_bass_kernel_spmd

    w1 = np.asarray(inputs["W_top1"])
    rows = pair_rows()
    w1p = np.zeros((KP * P, N1), w1.dtype)
    w1p[rows >= 0] = w1[rows[rows >= 0]]
    arrays = {
        "dense": inputs["r_dense_features"], "ids": inputs["ids"],
        **{f"tbl_{f}": inputs[f"tbl_{f}"] for f in range(NE)},
        "w1p": w1p, "w1a": w1[0:D], "w1b": w1[w1.shape[0] - D:],
        "b1": np.asarray(inputs["b_top1"]).reshape(M1, P).T,
        "w2": inputs["W_top2"], "b2": np.asarray(inputs["b_top2"]).reshape(M2, P).T,
        "w3": np.asarray(inputs["W_top3"]).reshape(M2, P).T,
    }
    arrays = {n: np.ascontiguousarray(a) for n, a in arrays.items()}
    nc = bacc.Bacc("TRN2", target_bir_lowering=False, num_devices=1)
    aps = {n: nc.dram_tensor(n, a.shape, mybir.dt.from_np(a.dtype), kind="ExternalInput").ap()
           for n, a in arrays.items()}
    out = nc.dram_tensor("out", (B, 1), F32, kind="ExternalOutput").ap()
    build(nc, aps["dense"], aps["ids"], [aps[f"tbl_{f}"] for f in range(NE)], aps["w1p"], aps["w1a"],
          aps["w1b"], aps["b1"], aps["w2"], aps["b2"], aps["w3"], out)
    return run_bass_kernel_spmd(nc, [arrays], core_ids=[0]).results[0]["out"]
```

```python
from contextlib import ExitStack

import numpy as np
import concourse.bass as bass
from concourse import mybir

F32 = mybir.dt.float32
F16 = mybir.dt.float16
BF16 = mybir.dt.bfloat16
I32 = mybir.dt.int32
ALU = mybir.AluOpType
ACT = mybir.ActivationFunctionType

B, D, NF = 2048, 128, 27
NE = NF - 1
P = 128
TILES = B // P
SLOTS = 32
NJ = NF - 1
Q, G = 4, P // 4
N1, N2 = 512, 256
PER_GROUP = 4
GROUPS = [range(a, min(a + PER_GROUP, NF)) for a in range(0, NF, PER_GROUP)]
NG = len(GROUPS)
VOCAB = [1250, 1250, 125000, 1000, 1000, 1000, 12500, 1250, 1000, 1250, 1000, 1000, 1250, 12500, 1250,
         12500, 1000, 1250, 1000, 1250, 12500, 1000, 1000, 12500, 1250, 12500]
VS = 1000
VC = 8
VP = VS // VC
IN_GROUP = [0, 1, 1, 1, 1, 1, 0]
LOOKUPS = sum(IN_GROUP)
HOT_GROUP = [g for g, n in enumerate(IN_GROUP) for _ in range(n)]
AHEAD = 3
RING = 2 * LOOKUPS
assert 2 * LOOKUPS % RING == 0


def place_features():
    looked = [f for f, v in enumerate(VOCAB) if v == VS][:LOOKUPS]
    rest = [-1] + [f for f in range(NE) if f not in looked]
    slots, order = [], iter(looked)
    for group, n in zip(GROUPS, IN_GROUP):
        for c in range(len(group)):
            slots.append((next(order) if c >= len(group) - n else rest.pop(0)) + 1)
    return slots, looked


SLOT_FEATURE, LOOKED = place_features()
FETCHED = [f for f in SLOT_FEATURE if f == 0 or f - 1 not in LOOKED]
GRAM_AT = [1, 2, 4, 5]
UNITS = 4
UG = G // UNITS
BG = UG // 2
RECTS = []
_at = 0
for _s in range(0, NJ, 3):
    _c = min(3, NJ - _s)
    RECTS.append((_s, _c, min(_s + 3, NJ), _at))
    _at += _c * RECTS[-1][2]
PAIRS = _at
KP = -(-PAIRS // P)
K1, K2 = KP + 1, N1 // P
M1, M2 = N1 // P, N2 // P
LOADS = 7


def pair_rows():
    rows = np.full(KP * P, -1, np.int64)
    for s, c, r, off in RECTS:
        for a in range(c):
            for i in range(r):
                j = s + a + 1
                if i < j:
                    x, y = sorted((SLOT_FEATURE[i], SLOT_FEATURE[j]))
                    rows[off + a * r + i] = D + x * NF - x * (x + 1) // 2 + y - x - 1
    return rows


def build(nc, dense, ids, ids_t, tables, w1p, w1a, w1b, b1, w2, b2, w3, out):
    with ExitStack() as ctx:
        def sb(name, shape, dt=F32):
            return ctx.enter_context(nc.sbuf_tensor(name, shape, dt))

        def sem(name):
            return ctx.enter_context(nc.semaphore(name))

        ident = sb("ident", [P, P])
        ids_sb = sb("ids_sb", [P, 2, NE], I32)
        emb = sb("emb", [P, 2, len(FETCHED), D])
        ids_all = sb("ids_all", [P, 2, LOOKUPS, P], I32)
        ids_16 = sb("ids_16", [P, 2, LOOKUPS, P], F16)
        row_of = sb("row_of", [P, VC, P], F16)
        stage = sb("stage", [P, 2, VC, D])
        rest = sb("rest", [P, 2, VC, D])
        parts = sb("parts", [P, LOOKUPS, 3, VC, D], BF16)
        onehot = sb("onehot", [P, RING, VC, P], BF16)
        xt = sb("xt", [P, 2, G, Q, SLOTS])
        dense_t = sb("dense_t", [P, 2, P])
        blocks = sb("blocks", [P, 2, G, NJ])
        turned = sb("turned", [P, NJ, SLOTS])
        pairs = sb("pairs", [P, 2, KP * P])
        pairs_t = sb("pairs_t", [P, KP, P])
        h1 = sb("h1", [P, M1, P])
        h2 = sb("h2", [P, M2, P])
        y_sb = sb("y_sb", [1, 2, P])
        w1_sb = sb("w1_sb", [P, K1, N1])
        w1b_sb = sb("w1b_sb", [P, N1])
        w2_sb = sb("w2_sb", [P, K2, N2])
        w3_sb = sb("w3_sb", [P, M2])
        b1_sb = sb("b1_sb", [P, M1])
        b2_sb = sb("b2_sb", [P, M2])

        pt = [ctx.enter_context(nc.psum_tensor(f"pt{k}", [P, PER_GROUP, P], F32)) for k in range(2)]
        pgram = ctx.enter_context(nc.psum_tensor("pgram", [P, 4, 512], F32))
        pmix = ctx.enter_context(nc.psum_tensor("pmix", [P, 512], F32))
        ph1 = ctx.enter_context(nc.psum_tensor("ph1", [P, M1, P], F32))
        ppairs = pmix[:, 0:KP * P].rearrange("p (k s) -> p k s", k=KP)
        ph2 = pmix[:, 0:N2].rearrange("p (m s) -> p m s", m=M2)
        py = pmix[0:1, KP * P:KP * P + P]

        s_zero = sem("s_zero")
        s_ident = sem("s_ident")
        s_weights = sem("s_weights")
        s_pads = sem("s_pads")
        s_w1 = sem("s_w1")
        s_ids = [sem(f"s_ids{k}") for k in range(2)]
        s_dense = [sem(f"s_dense{k}") for k in range(2)]
        s_ids_all = [sem(f"s_ids_all{k}") for k in range(2)]
        s_stage = [sem(f"s_stage{k}") for k in range(2)]
        s_row_of = sem("s_row_of")
        s_16 = sem("s_16")
        s_part = [sem(f"s_part{k}") for k in range(3)]
        s_rest = sem("s_rest")
        s_hot = sem("s_hot")
        s_rows = [[sem(f"s_rows{k}_{g}") for g in range(NG)] for k in range(2)]
        s_go = sem("s_go")
        s_turned = sem("s_turned")
        s_xt = sem("s_xt")
        s_dt = sem("s_dt")
        s_gram = sem("s_gram")
        s_blk = [sem("s_blk_dve"), sem("s_blk_act")]
        s_flip = sem("s_flip")
        s_pick = [sem("s_pick_dve"), sem("s_pick_act")]
        s_pp = sem("s_pp")
        s_pe = sem("s_pe")
        s_l1 = sem("s_l1")
        s_r1 = sem("s_r1")
        s_l2 = sem("s_l2")
        s_r2 = sem("s_r2")
        s_l3 = sem("s_l3")
        s_y = sem("s_y")
        s_out = [sem("s_out0"), sem("s_out1")]

        block = ctx.enter_context(nc.Block())

        def fetched(group):
            return [SLOT_FEATURE[slot] for slot in group if SLOT_FEATURE[slot] in FETCHED]

        def steps(eng, step):
            step(0, 0, True, False, False)
            step(0, 1, True, True, False)
            step(1, 0, True, True, True)
            step(1, 1, True, True, True)
            with eng.Fori(2, TILES // 2 - 1) as i:
                step(i, 0, True, True, True)
                step(i, 1, True, True, True)
            step(TILES // 2 - 1, 0, True, True, True)
            step(TILES // 2 - 1, 1, True, True, True)
            step(TILES // 2, 0, False, True, True)
            step(TILES // 2, 1, False, False, True)

        def following(i, k):
            if isinstance(i, int) and 2 * i + k == TILES - 1:
                return None
            return i + (k + 1) // 2, (k + 1) % 2

        def back(i, k, n):
            return i + (k - n) // 2, (k - n) % 2

        def wait(eng, s, value):
            if not isinstance(value, int) or value > 0:
                eng.wait_ge(s, value)

        @block.sync
        def _(sp):
            def load(i, k):
                if not isinstance(i, int) or i > 0:
                    sp.wait_ge(s_turned, NG * (2 * i + k - 1))
                sp.dma_start(ids_sb[:, k, :], ids[bass.ts(2 * i + k, P), :]).then_inc(s_ids[k], 16)
                sp.dma_start(emb[:, k, 0, :], dense[bass.ts(2 * i + k, P), :]).then_inc(s_dense[k], 16)
                sp.dma_start(ids_all[:, k, :, :], ids_t[:, bass.ts(2 * i + k, P)].partition_broadcast(P)
                             ).then_inc(s_ids_all[k], 16)

            def load_table(n):
                if n >= 2:
                    sp.wait_ge(s_rest, n - 1)
                sp.dma_start(stage[0:VP, n % 2, :, :],
                             tables[LOOKED[n]].rearrange("(p c) d -> p c d", c=VC)).then_inc(s_stage[n % 2], 16)

            def store(i, k):
                sp.wait_ge(s_y, 2 * i + k + 1)
                sp.dma_start(out[bass.ts(2 * i + k, P), :].rearrange("s o -> o s"),
                             y_sb[:, k, :]).then_inc(s_out[k], 16)

            load(0, 0)
            for n in range(2):
                load_table(n)
            load(0, 1)
            for n in range(2, LOOKUPS):
                load_table(n)
            loads = [(w1_sb[:, 0:KP, :], w1p.rearrange("(c p) n -> p c n", p=P)),
                     (w1_sb[:, KP, :], w1a), (w1b_sb[:], w1b),
                     (w2_sb[:], w2.rearrange("(c p) n -> p c n", p=P)),
                     (w3_sb[:], w3), (b1_sb[:], b1), (b2_sb[:], b2)]
            assert len(loads) == LOADS
            for dst, src in loads:
                sp.dma_start(dst, src).then_inc(s_weights, 16)
            load(1, 0)
            load(1, 1)
            store(0, 0)
            with sp.Fori(2, TILES // 2) as i:
                load(i, 0)
                store(i - 2, 1)
                load(i, 1)
                store(i - 1, 0)
            store(TILES // 2 - 2, 1)
            store(TILES // 2 - 1, 0)
            store(TILES // 2 - 1, 1)
            for s in s_out:
                sp.wait_ge(s, 16 * (TILES // 2))

        @block.gpsimd
        def _(pool):
            pool.memset(ident[:], 0.0).then_inc(s_zero, 1)
            pool.wait_ge(s_zero, 1)
            pool.affine_select(out=ident[:], in_=ident[:], compare_op=ALU.not_equal, fill=1.0, base=0,
                               pattern=[[-1, P]], channel_multiplier=1).then_inc(s_ident, 1)
            pool.iota(row_of[:], pattern=[[1, VC], [0, P]], base=0, channel_multiplier=VC,
                      allow_small_or_imprecise_dtypes=True).then_inc(s_row_of, 1)

            def gather(i, k):
                pool.wait_ge(s_ids[k], 16 * (i + 1))
                pool.sem_inc(s_go, 1)
                for g, group in enumerate(GROUPS):
                    if not isinstance(i, int) or i > 0:
                        pool.wait_ge(s_turned, NG * (2 * i + k - 2) + g + 1)
                        pool.sem_inc(s_go, 1)
                    for f in fetched(group):
                        if f:
                            pool.indirect_dma_start(
                                out=emb[:, k, FETCHED.index(f), :], out_offset=None, in_=tables[f - 1],
                                in_offset=bass.IndirectOffsetOnAxis(ap=ids_sb[:, k, f - 1:f], axis=0),
                            ).then_inc(s_rows[k][g], 16)

            gather(0, 0)
            gather(0, 1)
            with pool.Fori(1, TILES // 2) as i:
                gather(i, 0)
                gather(i, 1)

        @block.tensor
        def _(pe):
            def turn(i, k, g):
                n = NG * k + g
                rows = fetched(GROUPS[g])
                pe.wait_ge(s_rows[k][g], 16 * sum(f > 0 for f in rows) * (i + 1))
                if g == 0:
                    pe.wait_ge(s_dense[k], 16 * (i + 1))
                wait(pe, s_xt, NG * 2 * i + n - 1)
                for c, f in enumerate(rows):
                    last = pe.transpose(pt[n % 2][:, c, :], emb[:, k, FETCHED.index(f), :], ident[:])
                for c in range(IN_GROUP[g]):
                    table = sum(IN_GROUP[:g]) + c
                    n_hot = LOOKUPS * k + table
                    pe.wait_ge(s_hot, 2 * LOOKUPS * i + n_hot + 1)
                    if isinstance(i, int) and (i, k) == (0, 0):
                        pe.wait_ge(s_part[2], table + 1)
                    for part in range(3):
                        for v in range(VC):
                            last = pe.matmul(pt[n % 2][:, len(rows) + c, :], parts[0:VP, table, part, v, :],
                                             onehot[0:VP, n_hot % RING, v, :],
                                             start=(part == 0 and v == 0), stop=(part == 2 and v == VC - 1))
                last.then_inc(s_turned, 1)

            def gram(i, k, u):
                if u == 0:
                    pe.wait_ge(s_xt, NG * (2 * i + k + 1))
                for s in s_blk:
                    wait(pe, s, UNITS * (2 * i + k) + u - 1)
                for c in range(UG):
                    bank = 2 * (u % 2) + c // BG
                    at = (c % BG) * Q * NJ
                    four = xt[:, k, u * UG + c, :, :]
                    last = pe.matmul(pgram[:, bank, at:at + Q * NJ], four.rearrange("p q f -> p (q f)"),
                                     four[:, :, 1:NF], start=True, stop=True)
                last.then_inc(s_gram, 1)

            def turn_pairs(i, k):
                for s in s_pick:
                    pe.wait_ge(s, 2 * i + k + 1)
                wait(pe, s_y, 2 * i + k)
                for c in range(KP):
                    last = pe.transpose(ppairs[:, c, :], pairs[:, k, bass.ts(c, P)], ident[:])
                last.then_inc(s_pp, 1)

            def layer1(i, k):
                pe.wait_ge(s_pe, 2 * i + k + 1)
                pe.wait_ge(s_dt, 2 * i + k + 1)
                if isinstance(i, int) and (i, k) == (0, 0):
                    pe.wait_ge(s_weights, 16 * LOADS)
                    pe.wait_ge(s_w1, 1)
                for m in range(M1):
                    for c in range(K1):
                        rhs = pairs_t[:, c, :] if c < KP else dense_t[:, k, :]
                        last = pe.matmul(ph1[:, m, :], w1_sb[:, c, bass.ts(m, P)], rhs,
                                         start=(c == 0), stop=(c == K1 - 1))
                last.then_inc(s_l1, 1)

            def layer2(i, k):
                pe.wait_ge(s_r1, 2 * i + k + 1)
                for m in range(M2):
                    for c in range(K2):
                        last = pe.matmul(ph2[:, m, :], w2_sb[:, c, bass.ts(m, P)], h1[:, c, :],
                                         start=(c == 0), stop=(c == K2 - 1))
                last.then_inc(s_l2, 1)

            def layer3(i, k):
                pe.wait_ge(s_r2, 2 * i + k + 1)
                for c in range(M2):
                    last = pe.matmul(py, w3_sb[:, c:c + 1], h2[:, c, :], start=(c == 0), stop=(c == M2 - 1))
                last.then_inc(s_l3, 1)

            def step(i, k, tile, gram_, mlp):
                for g in range(NG):
                    if tile:
                        turn(i, k, g)
                    if mlp and g == 2:
                        turn_pairs(*back(i, k, 2))
                    if mlp and g == 3:
                        layer1(*back(i, k, 2))
                    if mlp and g == 5:
                        layer2(*back(i, k, 2))
                    if gram_ and g in GRAM_AT:
                        gram(*back(i, k, 1), GRAM_AT.index(g))
                    if mlp and g == 6:
                        layer3(*back(i, k, 2))

            pe.wait_ge(s_ident, 1)
            pe.wait_ge(s_pads, 3)
            steps(pe, step)

        def copy_blocks(eng, copy, i, k, u, half):
            eng.wait_ge(s_gram, UNITS * (2 * i + k) + u + 1)
            if u == 0:
                wait(eng, s_flip, 2 * i + k - 1)
            for q in (2 * half, 2 * half + 1):
                rows = slice(SLOTS * q, SLOTS * q + SLOTS)
                src = pgram[rows, 2 * (u % 2):2 * (u % 2) + 2, 0:BG * Q * NJ]
                src = src.rearrange("p b (c q j) -> p b c q j", c=BG, q=Q)[:, :, :, q, :]
                dst = blocks[rows, k, u * UG:(u + 1) * UG, :].rearrange("p (b c) j -> p b c j", b=2)
                last = copy(dst, src)
            last.then_inc(s_blk[half], 1)

        def pick(eng, copy, i, k, rects, engine):
            eng.wait_ge(s_flip, 2 * i + k + 1)
            wait(eng, s_pp, 2 * i + k - 1)
            for s, c, r, off in rects:
                last = copy(pairs[:, k, off:off + c * r].rearrange("p (c r) -> p c r", c=c),
                            turned[:, s:s + c, 0:r])
            last.then_inc(s_pick[engine], 1)

        @block.vector
        def _(dve):
            def copy(dst, src):
                return dve.tensor_copy(dst, src)

            def split_tables(g):
                for n in [n for n in range(LOOKUPS) if HOT_GROUP[n] == g]:
                    for m in ([0] if n == 0 else []) + ([n + 1] if n + 1 < LOOKUPS else []):
                        dve.wait_ge(s_part[0], m + 1)
                        if m >= 2:
                            dve.wait_ge(s_part[2], m - 1)
                        dve.tensor_tensor(rest[0:VP, m % 2, :, :], stage[0:VP, m % 2, :, :],
                                          parts[0:VP, m, 0, :, :], ALU.subtract).then_inc(s_rest, 1)
                    dve.wait_ge(s_part[1], n + 1)
                    dve.tensor_tensor(parts[0:VP, n, 2, :, :], rest[0:VP, n % 2, :, :],
                                      parts[0:VP, n, 1, :, :], ALU.subtract).then_inc(s_part[2], 1)

            def make_hot(i, k, g):
                for c in range(IN_GROUP[g]):
                    table = sum(IN_GROUP[:g]) + c
                    used = table - RING
                    pair, parity = back(i, k, -(used // LOOKUPS))
                    if not isinstance(i, int) or 2 * pair + parity >= 0:
                        dve.wait_ge(s_turned, NG * (2 * pair + parity) + HOT_GROUP[used % LOOKUPS] + 1)
                    n_hot = LOOKUPS * k + table
                    dve.tensor_tensor(onehot[0:VP, n_hot % RING, :, :],
                                      ids_16[0:VP, k, table, :].unsqueeze(1).to_broadcast([VP, VC, P]),
                                      row_of[0:VP, :, :],
                                      ALU.is_equal).then_inc(s_hot, 1)

            def flip(i, k):
                for s in s_blk:
                    dve.wait_ge(s, UNITS * (2 * i + k + 1))
                for s in s_pick:
                    wait(dve, s, 2 * i + k)
                dve.transpose(turned[:], blocks[:, k, :, :].rearrange("p g j -> p j g")).then_inc(s_flip, 1)

            def copy_dense(i, k):
                dve.wait_ge(s_xt, NG * (2 * i + k + 1))
                wait(dve, s_l1, 2 * i + k - 1)
                copy(dense_t[:, k, :].rearrange("p (q g) -> p q g", q=Q),
                     xt[:, k, :, :, 0].rearrange("p g q -> p q g")).then_inc(s_dt, 1)

            def relu2(i, k):
                dve.wait_ge(s_l2, 2 * i + k + 1)
                wait(dve, s_l3, 2 * i + k)
                for m in range(M2):
                    last = dve.tensor_scalar(h2[:, m, :], ph2[:, m, :], b2_sb[:, m:m + 1], 0.0, ALU.add, ALU.max)
                last.then_inc(s_r2, 1)

            def put_y(i, k):
                dve.wait_ge(s_l3, 2 * i + k + 1)
                wait(dve, s_out[k], 16 * i)
                copy(y_sb[:, k, :], py).then_inc(s_y, 1)

            def step(i, k, tile, gram, mlp):
                first = isinstance(i, int) and (i, k) == (0, 0)
                if first:
                    dve.wait_ge(s_16, 1)
                    for g in range(AHEAD):
                        split_tables(g)
                        make_hot(i, k, g)
                for g in range(NG):
                    if tile and g + AHEAD < NG:
                        if first:
                            split_tables(g + AHEAD)
                        make_hot(i, k, g + AHEAD)
                    elif tile and following(i, k):
                        if g + AHEAD == NG:
                            dve.wait_ge(s_16, 2 * i + k + 2)
                        make_hot(*following(i, k), g + AHEAD - NG)
                    if mlp and g == 5:
                        relu2(*back(i, k, 2))
                    if gram and g in GRAM_AT:
                        copy_blocks(dve, copy, *back(i, k, 1), GRAM_AT.index(g), 0)
                    if gram and g == 6:
                        if isinstance(i, int) and (i, k) == (0, 1):
                            dve.wait_ge(s_weights, 16 * LOADS)
                            dve.tensor_tensor(w1_sb[:, KP, :], w1_sb[:, KP, :], w1b_sb[:],
                                              ALU.add).then_inc(s_w1, 1)
                        flip(*back(i, k, 1))
                        pick(dve, copy, *back(i, k, 1), RECTS[0::2], 0)
                        copy_dense(*back(i, k, 1))
                    if mlp and g == 6:
                        put_y(*back(i, k, 2))

            dve.memset(xt[:, :, :, :, NF:SLOTS].rearrange("p k g q f -> p (k g q) f"), 0.0).then_inc(s_pads, 1)
            for k in range(2):
                dve.memset(pairs[:, k, PAIRS:KP * P], 0.0).then_inc(s_pads, 1)
            dve.wait_ge(s_row_of, 1)
            steps(dve, step)

        @block.scalar
        def _(act):
            def copy(dst, src):
                return act.activation(dst, src, ACT.Copy)

            def copy_pairs(i, k):
                act.wait_ge(s_pp, 2 * i + k + 1)
                wait(act, s_l1, 2 * i + k)
                copy(pairs_t[:], ppairs).then_inc(s_pe, 1)

            def relu1(i, k):
                act.wait_ge(s_l1, 2 * i + k + 1)
                wait(act, s_l2, 2 * i + k)
                for m in range(M1):
                    last = act.activation(h1[:, m, :], ph1[:, m, :], ACT.Relu, bias=b1_sb[:, m:m + 1])
                last.then_inc(s_r1, 1)

            def round_table(n):
                act.wait_ge(s_stage[n % 2], 16 * (n // 2 + 1))
                copy(parts[0:VP, n, 0, :, :], stage[0:VP, n % 2, :, :]).then_inc(s_part[0], 1)

            def round_rest(n):
                act.wait_ge(s_rest, n + 1)
                copy(parts[0:VP, n, 1, :, :], rest[0:VP, n % 2, :, :]).then_inc(s_part[1], 1)

            def shrink_ids(i, k):
                act.wait_ge(s_ids_all[k], 16 * (i + 1))
                wait(act, s_hot, LOOKUPS * (2 * i + k - 1))
                copy(ids_16[:, k, :, :], ids_all[:, k, :, :]).then_inc(s_16, 1)

            def copy_group(i, k, g):
                group = GROUPS[g]
                act.wait_ge(s_turned, NG * (2 * i + k) + g + 1)
                if g == 0 and (not isinstance(i, int) or i > 0):
                    act.wait_ge(s_gram, UNITS * (2 * i + k - 1))
                    act.wait_ge(s_dt, 2 * i + k - 1)
                copy(xt[:, k, :, :, group[0]:group[-1] + 1].rearrange("p g q f -> p q g f"),
                     pt[(NG * k + g) % 2][:, 0:len(group), :].rearrange("p f (q g) -> p q g f", q=Q)
                     ).then_inc(s_xt, 1)

            def step(i, k, tile, gram, mlp):
                if isinstance(i, int) and (i, k) == (0, 0):
                    shrink_ids(0, 0)
                for g in range(NG):
                    if tile and g == 2 and following(i, k):
                        shrink_ids(*following(i, k))
                    if isinstance(i, int) and (i, k) == (0, 0):
                        for table in range(LOOKUPS):
                            if HOT_GROUP[table] == g + AHEAD or g == 0 and HOT_GROUP[table] < AHEAD:
                                if table == 0:
                                    round_table(0)
                                if table + 1 < LOOKUPS:
                                    round_table(table + 1)
                                round_rest(table)
                    if tile:
                        copy_group(i, k, g)
                    if mlp and g == 2:
                        copy_pairs(*back(i, k, 2))
                    if gram and g in GRAM_AT:
                        copy_blocks(act, copy, *back(i, k, 1), GRAM_AT.index(g), 1)
                    if mlp and g == 3:
                        relu1(*back(i, k, 2))
                    if gram and g == 6:
                        pick(act, copy, *back(i, k, 1), RECTS[1::2], 1)

            steps(act, step)


def kernel(**inputs):
    import concourse.bacc as bacc
    from concourse.bass_utils import run_bass_kernel_spmd

    w1 = np.asarray(inputs["W_top1"])
    rows = pair_rows()
    w1p = np.zeros((KP * P, N1), w1.dtype)
    w1p[rows >= 0] = w1[rows[rows >= 0]]
    arrays = {
        "dense": inputs["r_dense_features"], "ids": inputs["ids"],
        "ids_t": np.asarray(inputs["ids"])[:, LOOKED].T,
        **{f"tbl_{f}": inputs[f"tbl_{f}"] for f in range(NE)},
        "w1p": w1p, "w1a": w1[0:D], "w1b": w1[w1.shape[0] - D:],
        "b1": np.asarray(inputs["b_top1"]).reshape(M1, P).T,
        "w2": inputs["W_top2"], "b2": np.asarray(inputs["b_top2"]).reshape(M2, P).T,
        "w3": np.asarray(inputs["W_top3"]).reshape(M2, P).T,
    }
    arrays = {n: np.ascontiguousarray(a) for n, a in arrays.items()}
    nc = bacc.Bacc("TRN2", target_bir_lowering=False, num_devices=1)
    aps = {n: nc.dram_tensor(n, a.shape, mybir.dt.from_np(a.dtype), kind="ExternalInput").ap()
           for n, a in arrays.items()}
    out = nc.dram_tensor("out", (B, 1), F32, kind="ExternalOutput").ap()
    build(nc, aps["dense"], aps["ids"], aps["ids_t"], [aps[f"tbl_{f}"] for f in range(NE)], aps["w1p"], aps["w1a"],
          aps["w1b"], aps["b1"], aps["w2"], aps["b2"], aps["w3"], out)
    return run_bass_kernel_spmd(nc, [arrays], core_ids=[0]).results[0]["out"]
```
